# Optimizing a Trainium2 kernel written in Bass

```python
import numpy as np
import jax
import jax.numpy as jnp

def _softmax(x, axis=-1):
    return jax.nn.softmax(x, axis=axis)
def _gelu(x):
    return jax.nn.gelu(x, approximate=True)
def _silu(x):
    return jax.nn.silu(x)
def _sigmoid(x):
    return jax.nn.sigmoid(x)
def _layernorm(x, axis=-1, eps=1e-5):
    m = jnp.mean(x, axis=axis, keepdims=True)
    v = jnp.var(x, axis=axis, keepdims=True)
    return (x - m) / jnp.sqrt(v + eps)
def _scatter_add(tgt, idx, src, axis=0):
    return tgt.at[idx].add(src)
def _segment_sum(src, seg, n):
    return jax.ops.segment_sum(src, seg, n)

kernel_name = 'mk_adj_preln_d2_adj_256_83421f'

def setup_inputs(seed: int = 0):
    np.random.seed(seed)
    _w = jnp.asarray
    def _rec_inputs():
        import jax
        import jax.numpy as jnp
        _gk = jax.random.key(seed)
        x = -0.0005207 + 1.001 * jax.random.normal(jax.random.fold_in(_gk, 1), (8, 2048, 256), jnp.float32)
        _a = jax.random.bernoulli(jax.random.fold_in(_gk, 2), 0.015625, (2048, 2048))
        _a = jnp.logical_or(_a, jnp.swapaxes(_a, -1, -2))
        _a = jnp.logical_or(_a, jnp.eye(2048, dtype=bool))
        adj = _a.astype(jnp.int32)
        return x, adj
    x, adj = _rec_inputs()
    def _L0_gnn_setup():
        import jax, jax.numpy as jnp
        import numpy as np
        import math
        CHUNK = 256
        NUM_HEADS = 4
        EPS = 1e-05
        key = jax.random.key(seed)
        ks = jax.random.split(key, 12)
        B, N, F = (4, 2048, 256)
        x = jax.random.normal(ks[0], (B, N, F), dtype=jnp.float32)
        adj_matrix = jax.random.randint(ks[1], (N, N), 0, 2, dtype=jnp.int32)
        s = 1.0 / math.sqrt(F)
        Wq = jax.random.normal(ks[2], (F, F), dtype=jnp.float32) * s
        bq = jnp.zeros((F,), dtype=jnp.float32)
        Wk = jax.random.normal(ks[3], (F, F), dtype=jnp.float32) * s
        bk = jnp.zeros((F,), dtype=jnp.float32)
        Wv = jax.random.normal(ks[4], (F, F), dtype=jnp.float32) * s
        bv = jnp.zeros((F,), dtype=jnp.float32)
        Wo = jax.random.normal(ks[5], (F, F), dtype=jnp.float32) * s
        bo = jnp.zeros((F,), dtype=jnp.float32)
        gamma = jnp.ones((F,), dtype=jnp.float32)
        beta = jnp.zeros((F,), dtype=jnp.float32)
        return {'x': x, 'adj_matrix': adj_matrix, 'Wq': Wq, 'bq': bq, 'Wk': Wk, 'bk': bk, 'Wv': Wv, 'bv': bv, 'Wo': Wo, 'bo': bo, 'gamma': gamma, 'beta': beta}
    _L0_gnn_all = _L0_gnn_setup()
    _L0_gnn_in = {k: v for k, v in _L0_gnn_all.items() if k in ('Wq', 'bq', 'Wk', 'bk', 'Wv', 'bv', 'Wo', 'bo', 'gamma', 'beta', )}
    del _L0_gnn_all

    def _L1_gnn_setup():
        import jax, jax.numpy as jnp
        import numpy as np
        IN_DIM = 256
        OUT_DIM = 64
        NUM_HEADS = 4
        ALPHA = 0.2
        NEG_INF = -9000000000000000.0
        key = jax.random.key(seed)
        k1, k2, k3, k4 = jax.random.split(key, 4)
        B, N = (4, 2048)
        h = jax.random.normal(k1, (B, N, IN_DIM), dtype=jnp.float32)
        adj = jax.random.randint(k2, (N, N), 0, 2, dtype=jnp.int32)
        W = jax.random.normal(k3, (IN_DIM, NUM_HEADS * OUT_DIM), dtype=jnp.float32) * (1.0 / np.sqrt(IN_DIM))
        a = jax.random.normal(k4, (2 * OUT_DIM,), dtype=jnp.float32) * (1.0 / np.sqrt(2 * OUT_DIM))
        return {'h': h, 'adj': adj, 'W': W, 'a': a}
    _L1_gnn_all = _L1_gnn_setup()
    _L1_gnn_in = {k: v for k, v in _L1_gnn_all.items() if k in ('W', 'a', )}
    del _L1_gnn_all

    return {
        "x": x,
        "adj": adj,
        "L0_gnn_Wq": _L0_gnn_in["Wq"],
        "L0_gnn_bq": _L0_gnn_in["bq"],
        "L0_gnn_Wk": _L0_gnn_in["Wk"],
        "L0_gnn_bk": _L0_gnn_in["bk"],
        "L0_gnn_Wv": _L0_gnn_in["Wv"],
        "L0_gnn_bv": _L0_gnn_in["bv"],
        "L0_gnn_Wo": _L0_gnn_in["Wo"],
        "L0_gnn_bo": _L0_gnn_in["bo"],
        "L0_gnn_gamma": _L0_gnn_in["gamma"],
        "L0_gnn_beta": _L0_gnn_in["beta"],
        "L1_gnn_W": _L1_gnn_in["W"],
        "L1_gnn_a": _L1_gnn_in["a"],
    }

def reference(x, adj, L0_gnn_Wq, L0_gnn_bq, L0_gnn_Wk, L0_gnn_bk, L0_gnn_Wv, L0_gnn_bv, L0_gnn_Wo, L0_gnn_bo, L0_gnn_gamma, L0_gnn_beta, L1_gnn_W, L1_gnn_a):
    import jax
    import jax.numpy as jnp
    def _L0_gnn_ref(x, adj_matrix, Wq, bq, Wk, bk, Wv, bv, Wo, bo, gamma, beta):
        import jax, jax.numpy as jnp
        import numpy as np
        import math
        CHUNK = 256
        NUM_HEADS = 4
        EPS = 1e-05
        B, N, Fin = x.shape
        H = NUM_HEADS
        Dout = Wq.shape[0]
        Dh = Dout // H
        Nc = N // CHUNK
        q = (x @ Wq.T + bq).reshape(B, N, H, Dh).transpose(0, 2, 1, 3)
        k = (x @ Wk.T + bk).reshape(B, N, H, Dh).transpose(0, 2, 1, 3)
        v = (x @ Wv.T + bv).reshape(B, N, H, Dh).transpose(0, 2, 1, 3)
        kc = k.reshape(B, H, Nc, CHUNK, Dh)
        vc = v.reshape(B, H, Nc, CHUNK, Dh)
        scores = jnp.einsum('bhnd,bhjcd->bhnjc', q, kc) / jnp.sqrt(jnp.asarray(Dh, dtype=q.dtype))
        scores = jnp.clip(scores, -10.0, 10.0)
        mask = adj_matrix.reshape(N, Nc, CHUNK)[None, None]
        scores = jnp.where(mask == 0, jnp.asarray(-10.0, scores.dtype), scores)
        attn = jax.nn.softmax(scores, axis=-1)
        ctx = jnp.einsum('bhnjc,bhjcd->bhnd', attn, vc)
        ctx = ctx.transpose(0, 2, 1, 3).reshape(B, N, Dout)
        out = ctx @ Wo.T + bo
        out = out + x
        mu = jnp.mean(out, axis=-1, keepdims=True)
        var = jnp.mean(jnp.square(out - mu), axis=-1, keepdims=True)
        out = (out - mu) * jax.lax.rsqrt(var + EPS) * gamma + beta
        return out

    def _L1_gnn_ref(h, adj, W, a):
        import jax, jax.numpy as jnp
        import numpy as np
        IN_DIM = 256
        OUT_DIM = 64
        NUM_HEADS = 4
        ALPHA = 0.2
        NEG_INF = -9000000000000000.0
        B, N, _ = h.shape
        H, D = (NUM_HEADS, OUT_DIM)
        q = (h @ W).reshape(B, N, H, D)
        a_src, a_dst = (a[:D], a[D:])
        e_src = jnp.einsum('bnhd,d->bnh', q, a_src)
        e_dst = jnp.einsum('bnhd,d->bnh', q, a_dst)
        e = e_src[:, :, None, :] + e_dst[:, None, :, :]
        e = jnp.where(e >= 0, e, ALPHA * e)
        mask = (adj > 0)[None, :, :, None]
        e = jnp.where(mask, e, NEG_INF)
        attn = jax.nn.softmax(e, axis=2)
        h_prime = jnp.einsum('bijh,bjhd->bihd', attn, q)
        return jax.nn.elu(h_prime.reshape(B, N, H * D))

    h = jnp.maximum(_layernorm(x, axis=-1), 0.0)
    x = x + _L0_gnn_ref(h, adj, L0_gnn_Wq, L0_gnn_bq, L0_gnn_Wk, L0_gnn_bk, L0_gnn_Wv, L0_gnn_bv, L0_gnn_Wo, L0_gnn_bo, L0_gnn_gamma, L0_gnn_beta)
    h = jnp.maximum(_layernorm(x, axis=-1), 0.0)
    x = x + _L1_gnn_ref(h, adj, L1_gnn_W, L1_gnn_a)
    return x


_drawn_inputs = setup_inputs


def setup_inputs(seed=0):
    import zlib

    import numpy as np

    out = dict(_drawn_inputs(seed))
    spreads = {'L0_gnn_bq': (0.0, 0.8),
     'L0_gnn_bk': (0.0, 0.8),
     'L0_gnn_bv': (0.0, 0.1),
     'L0_gnn_bo': (0.0, 0.401),
     'L0_gnn_gamma': (1.0, 0.2),
     'L0_gnn_beta': (0.0, 0.1)}
    factors = {'L1_gnn_a': 4.396}
    for name, (base, spread) in spreads.items():
        noise = np.random.default_rng([zlib.crc32(name.encode()), seed]).standard_normal(out[name].shape)
        drawn = base * np.exp(spread * noise) if base else spread * noise
        out[name] = jnp.asarray(drawn.astype(out[name].dtype))
    for name, factor in factors.items():
        out[name] = (out[name] * factor).astype(out[name].dtype)
    return out
```

```python
import math
from contextlib import ExitStack

import concourse.bass as bass
from concourse import mybir

ALU = mybir.AluOpType
ACT = mybir.ActivationFunctionType
AX = mybir.AxisListType
F32 = mybir.dt.float32
F32R = mybir.dt.float32r
F16 = mybir.dt.float16
I32 = mybir.dt.int32
U8 = mybir.dt.uint8
RMAX = bass.bass_isa.ReduceOp.max

P = 128
B, N, F = 8, 2048, 256
H, D = 4, 64
E1 = D + 1
CHUNK = 256
NC = N // CHUNK
JC = CHUNK // P
NT = N // P
STRIP = 512
NS = N // STRIP
IT = STRIP // P
KC = F // P
STEPS = NC * H
EPS = 1e-5
CLIP = 10.0
SCALE = 1.0 / math.sqrt(D)
P_LOW = math.exp(-2 * CLIP)
LIFT = 10.0 * math.log(2.0)


def rows(ap):
    return ap.rearrange("(t p) f -> p t f", p=P)


def row_on_all(ap, n=P):
    return ap.rearrange("(o f) -> o f", o=1).to_broadcast([n, ap.shape[0]])


def pool_gate(nc, cell):
    nc.gpsimd.tensor_tensor(cell[:, 0:1], cell[:, 1:2], cell[:, 1:2], ALU.add)


def dve_gate(nc, cell):
    nc.vector.memset(cell[:, 0:1], 0.0)


def mask_block(nc, adj, ident16, mask8, mask_dram):
    with ExitStack() as ctx:
        sb = lambda name, shape, dt: ctx.enter_context(nc.sbuf_tensor(name, shape, dt))
        sem = lambda name: ctx.enter_context(nc.semaphore(name))
        adj_in = sb("adj_in", [P, 2, N], I32)
        adj16 = sb("adj16", [P, 2, N], F16)
        adj_t = [ctx.enter_context(nc.psum_tensor(f"adj_t{k}", [P, NT, P], F16)) for k in range(2)]
        adj_loaded = [sem("adj_loaded0"), sem("adj_loaded1")]
        ident_ready = sem("ident_ready")
        adj_cast = sem("adj_cast")
        adj_transposed = sem("adj_transposed")
        mask_written = sem("mask_written")
        mask_stored = sem("mask_stored")
        block = ctx.enter_context(nc.Block("mask_block"))
        adj_v = adj.rearrange("(i p) j -> i p j", p=P)

        @block.sync
        def _(sp):
            sp.sem_inc(adj_cast, 1)
            with sp.Fori(0, NT // 2) as m:
                for k in range(2):
                    sp.wait_ge(adj_cast, m * 2 + 1)
                    sp.dma_start(adj_in[:, k, :], adj_v[m * 2 + k]).then_inc(adj_loaded[k], 16)
            sp.wait_ge(mask_written, NT + 1)
            sp.dma_start(mask_dram, mask8[:, :, :]).then_inc(mask_stored, 16)
            sp.wait_ge(mask_stored, 16)

        @block.gpsimd
        def _(pool):
            nc.gpsimd.memset(ident16[:, :], 0.0).then_inc(ident_ready, 1)
            pool.wait_ge(ident_ready, 1)
            nc.gpsimd.affine_select(out=ident16[:, :], in_=ident16[:, :], compare_op=ALU.not_equal, fill=1.0,
                                    base=0, pattern=[[-1, P]], channel_multiplier=1).then_inc(ident_ready, 1)

        @block.vector
        def _(dve):
            dve.sem_inc(adj_transposed, 1)
            with dve.Fori(0, NT // 2) as m:
                for k in range(2):
                    dve.wait_ge(adj_loaded[k], (m + 1) * 16)
                    dve.wait_ge(adj_transposed, m * 2 + 1)
                    nc.vector.tensor_scalar(adj16[:, k, :], adj_in[:, k, :], 0.0, None, ALU.is_gt).then_inc(adj_cast, 1)

        @block.tensor
        def _(pe):
            pe.wait_ge(ident_ready, 2)
            pe.sem_inc(mask_written, 1)
            with pe.Fori(0, NT // 2) as m:
                for k in range(2):
                    pe.wait_ge(adj_cast, m * 2 + k + 2)
                    pe.wait_ge(mask_written, m * 2 + 1)
                    for jt in range(NT):
                        last = nc.tensor.transpose(adj_t[k][:, jt, :], adj16[:, k, jt * P:(jt + 1) * P], ident16[:, :])
                    last.then_inc(adj_transposed, 1)

        @block.scalar
        def _(act):
            with act.Fori(0, NT // 2) as m:
                for k in range(2):
                    act.wait_ge(adj_transposed, m * 2 + k + 2)
                    nc.scalar.activation(mask8[:, :, bass.ds((m * 2 + k) * P, P)], adj_t[k][:, :, :],
                                         ACT.Copy).then_inc(mask_written, 1)


T_USES, K_USES, V_USES = NT // 2, NS * H // 2, NT // 2
PROLOGUE_USES = T_USES + K_USES + V_USES
Q_USES = H // 2
STRIP_USES = Q_USES + STEPS + 2
BATCH_USES = PROLOGUE_USES + NS * STRIP_USES
SLOTS = 3
assert PROLOGUE_USES % SLOTS == 0 and STRIP_USES % SLOTS == 0
STRIP_ACTS = Q_USES + STEPS
BATCH_ACTS = K_USES + NS * STRIP_ACTS
PROBS = 4
LAG = 2
OUTS = 2


def layer0_block(nc, x, wq_t, bq, wk_t, bk, wv_t, bv, wo_t, bo, gamma, beta, x1, mask8):
    with ExitStack() as ctx:
        sb = lambda name, shape, dt=F32: ctx.enter_context(nc.sbuf_tensor(name, shape, dt))
        ps = lambda name, shape, dt=F32: ctx.enter_context(nc.psum_tensor(name, shape, dt))
        sem = lambda name: ctx.enter_context(nc.semaphore(name))

        wq_s = sb("wq_s", [P, KC, H, 2, D])
        wk_s = sb("wk_s", [P, KC, H, 2, D])
        wv_s = sb("wv_s", [P, KC, F])
        wo_s = sb("wo_s", [P, KC, F])
        bq_s = sb("bq_s", [P, H])
        bk_s = sb("bk_s", [P, H])
        bv_s = sb("bv_s", [P, F])
        bo_s = sb("bo_s", [P, F])
        gamma_s = sb("gamma_s", [P, F])
        beta_s = sb("beta_s", [P, F])
        ident = sb("ident", [P, P])
        low = sb("low", [P, 1])
        shift = sb("shift", [P, 1])
        neg_half = sb("neg_half", [P, NT])
        eps_s = sb("eps_s", [P, NT])

        pool_cell = sb("pool_cell", [P, 2])
        dve_cell = sb("dve_cell", [P, 1])
        xs = sb("xs", [P, NT, F])
        hs = sb("hs", [P, NT, F])
        h_t = sb("h_t", [P, KC, N])
        stats = sb("stats", [P, NT, 6])
        moments = sb("moments", [P, NT, 2])
        rstd = sb("rstd", [P, NT])
        k_hl = sb("k_hl", [P, H, N], F32R)
        q_hi = sb("q_hi", [P, H, STRIP], F32R)
        q_lo = sb("q_lo", [P, H, STRIP], F32R)
        v_w = H * E1 + P - E1
        v_s = sb("v_s", [P, NT, v_w])
        bound = sb("bound", [P, 2, JC, STRIP])
        probs = sb("probs", [P, PROBS, JC, STRIP])
        inv = sb("inv", [P, 2, IT])
        ctx_part = sb("ctx_part", [P, H, IT, D])
        ctx_sum = sb("ctx_sum", [P, IT, H, D])
        ctx_t = sb("ctx_t", [P, KC, STRIP])
        y = sb("y", [P, IT, F])
        y_stats = sb("y_stats", [P, IT, 6])
        y_moments = sb("y_moments", [P, IT, 2])
        y_rstd = sb("y_rstd", [P, IT])

        slots = [ps(f"slot{k}", [P, 2, STRIP]) for k in range(SLOTS)]
        outs = [ps(f"outs{k}", [P, IT, P]) for k in range(OUTS)]

        consts_loaded = sem("consts_loaded")
        consts_ready = sem("consts_ready")
        x_loaded = sem("x_loaded")
        stats_done = sem("stats_done")
        moments_done = sem("moments_done")
        var_eps_done = sem("var_eps_done")
        rstd_done = sem("rstd_done")
        norm_x_done = sem("norm_x_done")
        h_relu_done = sem("h_relu_done")
        h_res_done = sem("h_res_done")
        slot_filled = sem("slot_filled")
        slot_free = sem("slot_free")
        act_done = sem("act_done")
        bound_ready = sem("bound_ready")
        probs_used = sem("probs_used")
        inv_done = sem("inv_done")
        ctx_scaled = sem("ctx_scaled")
        ctx_added = sem("ctx_added")
        y_stats_done = sem("y_stats_done")
        y_moments_done = sem("y_moments_done")
        y_chain = sem("y_chain")
        x1_stored = sem("x1_stored")

        def t_use(k):
            return k

        def k_use(s, hp):
            return T_USES + s * (H // 2) + hp

        def v_use(k):
            return T_USES + K_USES + k

        Y_CHAIN = 7

        consts = [(wv_s[:, :, :], wv_t.rearrange("(c p) o -> p c o", p=P)),
                  (wo_s[:, :, :], wo_t.rearrange("(c p) o -> p c o", p=P)),
                  (bv_s[:, :], row_on_all(bv)), (bo_s[:, :], row_on_all(bo)),
                  (gamma_s[:, :], row_on_all(gamma)), (beta_s[:, :], row_on_all(beta))]
        for half in range(2):
            for w, w_dram in ((wq_s, wq_t), (wk_s, wk_t)):
                for c in range(KC):
                    consts.append((w[:, c, :, half, :],
                                   w_dram[c * P:(c + 1) * P, :].rearrange("p (h d) -> p h d", h=H)))
            for b_s, b_dram in ((bq_s, bq), (bk_s, bk)):
                consts.append((b_s[half * D:(half + 1) * D, :], b_dram))

        block = ctx.enter_context(nc.Block("layer0_block"))

        @block.sync
        def _(sp):
            for s in range(NS):
                sp.dma_start(xs[:, s * IT:(s + 1) * IT, :], rows(x[0])[:, s * IT:(s + 1) * IT, :]).then_inc(x_loaded, 16)

            def store(g, s, x1_b):
                sp.wait_ge(y_chain, (g + 1) * Y_CHAIN)
                sp.dma_start(rows(x1_b)[:, bass.ds(s * IT, IT), :], y[:, :, :]).then_inc(x1_stored, 16)

            with sp.Fori(0, B - 1) as b:
                with sp.Fori(0, NS) as s:
                    store(b * NS + s, s, x1[b])
                    sp.dma_start(xs[:, bass.ds(s * IT, IT), :], rows(x[b + 1])[:, bass.ds(s * IT, IT), :])\
                        .then_inc(x_loaded, 16)
            with sp.Fori(0, NS) as s:
                store((B - 1) * NS + s, s, x1[B - 1])
            sp.wait_ge(x1_stored, 16 * B * NS + 1)

        @block.gpsimd
        def _(pool):
            nc.gpsimd.memset(pool_cell[:, :], 0.0)
            nc.gpsimd.memset(low[:, :], P_LOW)
            nc.gpsimd.memset(shift[:, :], -CLIP)
            nc.gpsimd.memset(neg_half[:, :], -0.5)
            nc.gpsimd.memset(eps_s[:, :], EPS)
            nc.gpsimd.memset(ident[:, :], 0.0).then_inc(consts_ready, 1)
            pool.wait_ge(consts_ready, 1)
            nc.gpsimd.affine_select(out=ident[:, :], in_=ident[:, :], compare_op=ALU.not_equal, fill=1.0,
                                    base=0, pattern=[[-1, P]], channel_multiplier=1).then_inc(consts_ready, 1)
            for dst, src in consts:
                pool.dma_start(dst, src).then_inc(consts_loaded, 16)
            pool.wait_ge(consts_loaded, 16 * len(consts))
            with pool.Fori(0, B) as b:
                pool.wait_ge(moments_done, b + 1)
                nc.gpsimd.tensor_tensor(rstd[:, :], moments[:, :, 1], eps_s[:, :], ALU.add).then_inc(var_eps_done, 1)
                pool.wait_ge(var_eps_done, b + 1)
                nc.gpsimd.tensor_tensor(rstd[:, :], rstd[:, :], neg_half[:, :], ALU.pow).then_inc(rstd_done, 1)
                for k in range(T_USES):
                    pool.wait_ge(slot_filled, b * BATCH_USES + t_use(k) + 1)
                    pool_gate(nc, pool_cell)
                    pair = hs[:, 2 * k:2 * k + 2, :]
                    nc.gpsimd.tensor_scalar(pair, pair, 0.0, None, ALU.max).then_inc(h_relu_done, 1)
                    pool.wait_ge(h_relu_done, b * T_USES + k + 1)
                    nc.gpsimd.tensor_tensor(pair, pair, bo_s[:, :].unsqueeze(1).to_broadcast([P, 2, F]),
                                            ALU.add).then_inc(h_res_done, 1)
                with pool.Fori(0, NS) as s:
                    g = b * NS + s
                    for c in range(1, NC):
                        for h in range(H):
                            i = c * H + h
                            pool.wait_ge(ctx_scaled, b * (OUTS + NS * STEPS) + OUTS + s * STEPS + i + 1)
                            if c > 1:
                                pool.wait_ge(ctx_added, g * (STEPS - H) + i - 2 * H + 1)
                            nc.gpsimd.tensor_tensor(ctx_sum[:, :, h, :], ctx_sum[:, :, h, :], ctx_part[:, h, :, :],
                                                    ALU.add).then_inc(ctx_added, 1)
                    pool.wait_ge(y_moments_done, g + 1)
                    across = lambda v: v.unsqueeze(2).to_broadcast([P, IT, F])
                    along = lambda v: v.unsqueeze(1).to_broadcast([P, IT, F])
                    chain = [
                        (y_rstd[:, :], y_moments[:, :, 1], eps_s[:, 0:IT], ALU.add),
                        (y_rstd[:, :], y_rstd[:, :], neg_half[:, 0:IT], ALU.pow),
                        (y[:, :, :], y[:, :, :], across(y_moments[:, :, 0]), ALU.subtract),
                        (y[:, :, :], y[:, :, :], across(y_rstd[:, :]), ALU.mult),
                        (y[:, :, :], y[:, :, :], along(gamma_s[:, :]), ALU.mult),
                        (y[:, :, :], y[:, :, :], along(beta_s[:, :]), ALU.add),
                        (y[:, :, :], y[:, :, :], xs[:, bass.ds(s * IT, IT), :], ALU.add),
                    ]
                    assert len(chain) == Y_CHAIN
                    for k, (dst, a, c, op) in enumerate(chain):
                        if k:
                            pool.wait_ge(y_chain, g * Y_CHAIN + k)
                        nc.gpsimd.tensor_tensor(dst, a, c, op).then_inc(y_chain, 1)

        @block.tensor
        def _(pe):
            pe.wait_ge(consts_ready, 2)
            pe.wait_ge(consts_loaded, 16 * len(consts))

            def fill(u):
                pe.wait_ge(slot_free, u + 1)

            def freed(u):
                pe.wait_ge(slot_free, u + SLOTS + 1)

            with pe.Fori(0, B) as b:
                u0 = b * BATCH_USES
                for k in range(T_USES):
                    slot = slots[t_use(k) % SLOTS]
                    pe.wait_ge(norm_x_done, b * T_USES + k + 1)
                    fill(u0 + t_use(k))
                    for t in range(2):
                        for c in range(KC):
                            last = nc.tensor.transpose(slot[:, c, t * P:(t + 1) * P],
                                                       hs[:, 2 * k + t, c * P:(c + 1) * P], ident[:, :])
                    last.then_inc(slot_filled, 1)
                for s in range(NS):
                    for hp in range(H // 2):
                        slot = slots[k_use(s, hp) % SLOTS]
                        if hp == 0:
                            freed(u0 + t_use(2 * s + 1))
                        fill(u0 + k_use(s, hp))
                        for r in range(2):
                            for c in range(KC):
                                last = nc.tensor.matmul(slot[:, r, :], wk_s[:, c, 2 * hp + r, :, :],
                                                        h_t[:, c, s * STRIP:(s + 1) * STRIP],
                                                        start=(c == 0), stop=(c == KC - 1))
                        last.then_inc(slot_filled, 1)
                for k in range(V_USES):
                    slot = slots[v_use(k) % SLOTS]
                    fill(u0 + v_use(k))
                    for t in range(2):
                        for c in range(KC):
                            tile = 2 * k + t
                            last = nc.tensor.matmul(slot[:, t, 0:F], h_t[:, c, tile * P:(tile + 1) * P], wv_s[:, c, :],
                                                    start=(c == 0), stop=(c == KC - 1))
                            if k == V_USES - 1 and t == 0 and c == 0:
                                last.then_inc(probs_used, PROBS)
                    last.then_inc(slot_filled, 1)
                with pe.Fori(0, NS) as s:
                    us = u0 + PROLOGUE_USES + s * STRIP_USES
                    for qu in range(Q_USES):
                        slot = slots[qu % SLOTS]
                        fill(us + qu)
                        for r in range(2):
                            for c in range(KC):
                                last = nc.tensor.matmul(slot[:, r, :], wq_s[:, c, 2 * qu + r, :, :],
                                                        h_t[:, c, bass.ds(s * STRIP, STRIP)],
                                                        start=(c == 0), stop=(c == KC - 1))
                        last.then_inc(slot_filled, 1)

                    def scores(i):
                        c, h = divmod(i, H)
                        slot = slots[(Q_USES + i) % SLOTS]
                        if i == 0 or i == 2:
                            freed(us + h // 2)
                        fill(us + Q_USES + i)
                        for r in range(JC):
                            keys = k_hl[:, h, (c * JC + r) * P:(c * JC + r + 1) * P]
                            nc.tensor.matmul(slot[:, r, :], keys, q_hi[:, h, :], start=True, stop=False)
                            last = nc.tensor.matmul(slot[:, r, :], keys, q_lo[:, h, :], start=False, stop=True)
                        last.then_inc(slot_filled, 1)

                    def values(i):
                        c, h = divmod(i, H)
                        n = s * STEPS + i
                        freed(us + Q_USES + i)
                        pe.wait_ge(ctx_scaled, b * (OUTS + NS * STEPS) + n + 1)
                        for q in range(IT):
                            for r in range(JC):
                                last = nc.tensor.matmul(outs[i % OUTS][:, q, :], probs[:, i % PROBS, r, q * P:(q + 1) * P],
                                                        v_s[:, c * JC + r, h * E1:h * E1 + P],
                                                        start=(r == 0), stop=(r == JC - 1))
                        last.then_inc(probs_used, 1)

                    for i in range(STEPS + LAG):
                        if i < STEPS:
                            scores(i)
                        if i >= LAG:
                            values(i - LAG)
                    u = Q_USES + STEPS
                    slot = slots[u % SLOTS]
                    g = b * NS + s
                    pe.wait_ge(ctx_added, (g + 1) * (STEPS - H))
                    fill(us + u)
                    for c in range(KC):
                        for q in range(IT):
                            last = nc.tensor.transpose(slot[:, c, q * P:(q + 1) * P],
                                                       ctx_sum[:, q, 2 * c:2 * c + 2, :].rearrange("p h d -> p (h d)"),
                                                       ident[:, :])
                    last.then_inc(slot_filled, 1)
                    slot = slots[(u + 1) % SLOTS]
                    fill(us + u + 1)
                    freed(us + u)
                    for q in range(IT):
                        out = slot[:, q // 2, (q % 2) * F:(q % 2 + 1) * F]
                        for c in range(KC):
                            last = nc.tensor.matmul(out, ctx_t[:, c, q * P:(q + 1) * P], wo_s[:, c, :],
                                                    start=(c == 0), stop=(c == KC - 1))
                    last.then_inc(slot_filled, 1)

        @block.scalar
        def _(act):
            act.wait_ge(consts_ready, 2)
            act.wait_ge(consts_loaded, 16 * len(consts))
            with act.Fori(0, B) as b:
                u0 = b * BATCH_USES
                for s in range(NS):
                    for hp in range(H // 2):
                        slot = slots[k_use(s, hp) % SLOTS]
                        act.wait_ge(slot_filled, u0 + k_use(s, hp) + 1)
                        for r in range(2):
                            h = 2 * hp + r
                            last = nc.scalar.activation(k_hl[:, h, s * STRIP:(s + 1) * STRIP], slot[:, r, :],
                                                        ACT.Identity, bias=bk_s[:, h:h + 1])
                        last.then_inc(act_done, 1)
                with act.Fori(0, NS) as s:
                    us = u0 + PROLOGUE_USES + s * STRIP_USES
                    g = b * NS + s

                    def make_bound(c):
                        if c >= 2:
                            act.wait_ge(slot_free, us + Q_USES + (c - 1) * H + SLOTS)
                        nc.scalar.activation(bound[:, c % 2, :, :], mask8[:, c * JC:(c + 1) * JC, bass.ds(s * STRIP, STRIP)],
                                             ACT.Identity, bias=low[:, 0:1]).then_inc(bound_ready, 1)

                    for qu in range(Q_USES):
                        act.wait_ge(slot_filled, us + qu + 1)
                        for r in range(2):
                            h = 2 * qu + r
                            last = nc.scalar.activation(q_hi[:, h, :], slots[qu % SLOTS][:, r, :],
                                                        ACT.Identity, bias=bq_s[:, h:h + 1])
                        last.then_inc(act_done, 1)
                        if qu == 0:
                            make_bound(0)
                    make_bound(1)
                    for i in range(STEPS):
                        u = Q_USES + i
                        act.wait_ge(slot_filled, us + u + 1)
                        nc.scalar.activation(slots[u % SLOTS][:, :, :], slots[u % SLOTS][:, :, :], ACT.Exp,
                                             bias=shift[:, 0:1], scale=SCALE).then_inc(act_done, 1)
                        c, h = divmod(i, H)
                        if h == 1 and 2 <= c + 1 < NC:
                            make_bound(c + 1)

        @block.vector
        def _(dve):
            dve.wait_ge(consts_ready, 2)
            dve.wait_ge(consts_loaded, 16 * len(consts))
            dve.sem_inc(x1_stored, 1)
            nc.vector.memset(v_s[:, :, :], 1.0).then_inc(slot_free, SLOTS)
            with dve.Fori(0, B) as b:
                u0 = b * BATCH_USES
                a0 = b * BATCH_ACTS
                dve.wait_ge(x_loaded, (b + 1) * 16 * NS)
                for t in range(NT):
                    last = nc.vector.bn_stats(stats[:, t, :], xs[:, t, :])
                last.then_inc(stats_done, 1)
                dve.wait_ge(stats_done, b + 1)
                dve_gate(nc, dve_cell)
                for t in range(NT):
                    last = nc.vector.bn_aggr(moments[:, t, :], stats[:, t, :])
                last.then_inc(moments_done, 1)
                dve.wait_ge(moments_done, b + 1)
                dve.wait_ge(rstd_done, b + 1)
                for t in range(NT):
                    last = nc.vector.tensor_scalar(hs[:, t, :], xs[:, t, :], moments[:, t, 0:1], rstd[:, t:t + 1],
                                                   ALU.subtract, ALU.mult)
                    if t % 2:
                        last.then_inc(norm_x_done, 1)
                for k in range(T_USES):
                    dve.wait_ge(slot_filled, u0 + t_use(k) + 1)
                    nc.vector.tensor_scalar(h_t[:, :, 2 * k * P:(2 * k + 2) * P], slots[t_use(k) % SLOTS][:, :, 0:2 * P],
                                            0.0, None, ALU.max).then_inc(slot_free, 1)
                for s in range(NS):
                    for hp in range(H // 2):
                        slot = slots[k_use(s, hp) % SLOTS]
                        dve.wait_ge(act_done, a0 + s * (H // 2) + hp + 1)
                        for r in range(2):
                            h = 2 * hp + r
                            part = k_hl[D:P, h, s * STRIP:(s + 1) * STRIP]
                            last = nc.vector.scalar_tensor_tensor(part, slot[D:P, r, :], bk_s[D:P, h:h + 1],
                                                                  part.bitcast(F32), ALU.add, ALU.subtract)
                        last.then_inc(slot_free, 1)
                for k in range(V_USES):
                    dve.wait_ge(slot_filled, u0 + v_use(k) + 1)
                    slot = slots[v_use(k) % SLOTS]
                    for t in range(2):
                        last = nc.vector.tensor_tensor(
                            v_s[:, 2 * k + t, 0:H * E1].rearrange("p (h e) -> p h e", e=E1)[:, :, 0:D],
                            slot[:, t, 0:F].rearrange("p (h d) -> p h d", d=D),
                            bv_s[:, :].rearrange("p (h d) -> p h d", d=D), ALU.add)
                        if k == 0 and t == 0:
                            last.then_inc(ctx_scaled, OUTS)
                    last.then_inc(slot_free, 1)
                with dve.Fori(0, NS) as s:
                    g = b * NS + s
                    us = u0 + PROLOGUE_USES + s * STRIP_USES
                    acts = a0 + K_USES + s * STRIP_ACTS
                    used = b * (PROBS + NS * STEPS) + s * STEPS
                    for qu in range(Q_USES):
                        dve.wait_ge(act_done, acts + qu + 1)
                        for r in range(2):
                            h = 2 * qu + r
                            last = nc.vector.scalar_tensor_tensor(q_lo[:, h, :], slots[qu % SLOTS][:, r, :],
                                                                  bq_s[:, h:h + 1], q_hi[:, h, :].bitcast(F32),
                                                                  ALU.add, ALU.subtract)
                        last.then_inc(slot_free, 1)

                    def clip(i):
                        dve.wait_ge(act_done, acts + Q_USES + i + 1)
                        if i % H == 0:
                            dve.wait_ge(bound_ready, g * NC + i // H + 1)
                        dve.wait_ge(probs_used, used + i + 1)
                        nc.vector.scalar_tensor_tensor(probs[:, i % PROBS, :, :], slots[(Q_USES + i) % SLOTS][:, :, :],
                                                             P_LOW, bound[:, (i // H) % 2, :, :], ALU.max, ALU.min)\
                            .then_inc(slot_free, 1)

                    def invert(i):
                        dve.wait_ge(probs_used, used + PROBS + i + 1)
                        nc.vector.reciprocal(inv[:, i % 2, :], outs[i % OUTS][:, :, D]).then_inc(inv_done, 1)

                    def scale(i):
                        c, h = divmod(i, H)
                        dve.wait_ge(inv_done, g * STEPS + i + 1)
                        if c >= 2:
                            dve.wait_ge(ctx_added, g * (STEPS - H) + i - 2 * H + 1)
                        dst = ctx_sum[:, :, h, :] if c == 0 else ctx_part[:, h, :, :]
                        nc.vector.tensor_tensor(dst, outs[i % OUTS][:, :, 0:D],
                                                inv[:, i % 2, :].unsqueeze(2).to_broadcast([P, IT, D]),
                                                ALU.mult).then_inc(ctx_scaled, 1)

                    back = LAG + 1
                    for i in range(STEPS + back):
                        if i >= back:
                            invert(i - back)
                        if i < STEPS:
                            clip(i)
                        if i >= back:
                            scale(i - back)
                    u = Q_USES + STEPS
                    dve.wait_ge(slot_filled, us + u + 1)
                    nc.vector.tensor_copy(ctx_t[:, :, :], slots[u % SLOTS][:, :, :]).then_inc(slot_free, 1)
                    dve.wait_ge(slot_filled, us + u + 2)
                    dve.wait_ge(h_res_done, (b + 1) * T_USES)
                    dve.wait_ge(x1_stored, g * 16 + 1)
                    nc.vector.tensor_tensor(y[:, :, :].rearrange("p t f -> p (t f)"),
                                            slots[(u + 1) % SLOTS][:, :, :].rearrange("p r n -> p (r n)"),
                                            hs[:, bass.ds(s * IT, IT), :].rearrange("p t f -> p (t f)"),
                                            ALU.add).then_inc(slot_free, 1)
                    dve.wait_ge(slot_free, us + u + 2 + SLOTS)
                    for q in range(IT):
                        last = nc.vector.bn_stats(y_stats[:, q, :], y[:, q, :])
                    last.then_inc(y_stats_done, 1)
                    dve.wait_ge(y_stats_done, g + 1)
                    dve_gate(nc, dve_cell)
                    for q in range(IT):
                        last = nc.vector.bn_aggr(y_moments[:, q, :], y_stats[:, q, :])
                    last.then_inc(y_moments_done, 1)


WIDE = F + 2 * H
VW = 2 * E1
GROUPS = 4
GT = NT // GROUPS
UBUF = 8
PRE_USES = 2 * NT
SIDE_USES = PRE_USES + NS * IT
U_BATCH = UBUF + NS * H * NT


def layer1_block(nc, x1, w, a, out, mask_dram):
    with ExitStack() as ctx:
        sb = lambda name, shape, dt=F32: ctx.enter_context(nc.sbuf_tensor(name, shape, dt))
        ps = lambda name, shape, dt=F32: ctx.enter_context(nc.psum_tensor(name, shape, dt))
        sem = lambda name: ctx.enter_context(nc.semaphore(name))

        mask16 = sb("mask16", [P, NT, N], F16)
        w_s = sb("w_s", [P, KC, WIDE])
        a_s = sb("a_s", [P, 2, D])
        wa = sb("wa", [P, 2, KC, H, D])
        w_src_neg = sb("w_src_neg", [P, KC, H, P])
        ident1 = sb("ident1", [P, P])
        lift = sb("lift", [P, 1])
        zero = sb("zero", [P, 1])
        neg_half1 = sb("neg_half1", [P, NT])
        eps1 = sb("eps1", [P, NT])
        neg_one = sb("neg_one", [P, IT * H])

        pool_cell = sb("pool_cell1", [P, 2])
        dve_cell = sb("dve_cell1", [P, 1])
        xs = sb("x1_s", [P, NT, F])
        stats = sb("stats1", [P, NT, 6])
        moments = sb("moments1", [P, NT, 2])
        rstd = sb("rstd1", [P, NT])
        norm = sb("norm1", [P, 2, F])
        h_t = sb("h1_t", [P, KC, N])
        q_s = sb("q_s", [P, NT, WIDE])
        d_max = sb("d_max", [P, H])
        d_top = sb("d_top", [P, H])
        z = sb("z", [P, NT, H])
        z_neg = sb("z_neg", [P, NT, H])
        z_pos = sb("z_pos", [P, NT, H])
        d_rel = sb("d_rel", [P, NT, H])
        a_big = sb("a_big", [P, NT, H])
        a_small = sb("a_small", [P, NT, H])
        b_big = sb("b_big", [P, NT, H])
        b_small = sb("b_small", [P, NT, H])
        wv = sb("wv", [P, GT, H, VW])
        wv16 = sb("wv16", [P, NT, 2, H, VW], F16)
        u = sb("u", [P, UBUF, STRIP], F16)
        side_s = sb("side_s", [P, IT, H, E1])
        big_s = sb("big_s", [P, IT, H, E1])
        small_s = sb("small_s", [P, IT, H, E1])
        recip = sb("recip1", [P, IT * H])
        att = sb("att", [P, IT * H, D])
        e_att = sb("e_att", [P, IT * H, D])
        r_att = sb("r_att", [P, IT * H, D])

        s_rows = [ps(f"s_rows{k}", [P, STRIP]) for k in range(2)]
        sums = [ps(f"sums{k}", [P, STRIP]) for k in range(IT)]
        side = [ps(f"side{k}", [P, STRIP]) for k in range(2)]

        consts_loaded = sem("w_loaded")
        consts_ready = sem("consts1_ready")
        w_chain = sem("w_chain")
        mask_loaded = sem("mask_loaded")
        w_ready = sem("w_ready")
        x_loaded = sem("x1_loaded")
        stats_done = sem("stats1_done")
        moments_done = sem("moments1_done")
        var_eps_done = sem("var_eps1_done")
        rstd_done = sem("rstd1_done")
        norm_done = sem("norm1_done")
        side_filled = sem("side_filled")
        side_free = sem("side_free")
        d_max_done = sem("d_max_done")
        d_top_done = sem("d_top_done")
        zd_done = sem("zd_done")
        z_parts_done = sem("z_parts_done")
        ab_done = sem("ab_done")
        wv_q_done = sem("wv_q_done")
        wv_b_done = sem("wv_b_done")
        wv_high_done = sem("wv_high_done")
        wv_low_done = sem("wv_low_done")
        s_rows_filled = sem("s_rows_filled")
        u_ready = sem("u_ready")
        u_used = sem("u_used")
        sums_free = sem("sums_free")
        fin_chain = sem("fin_chain")
        elu_done = sem("elu_done")
        out_stored = sem("out_stored")

        FIN = 8
        consts = [(w_s[:, :, 0:F], w.rearrange("(c p) o -> p c o", p=P)),
                  (a_s[:, :, :].rearrange("p t d -> p (t d)"), row_on_all(a))]
        block = ctx.enter_context(nc.Block("layer1_block"))

        @block.sync
        def _(sp):
            for dst, src in consts:
                sp.dma_start(dst, src).then_inc(consts_loaded, 16)
            sp.dma_start(xs[:, :, :], rows(x1[0])).then_inc(x_loaded, 16)

            def store(g, s, out_b):
                sp.wait_ge(fin_chain, (g + 1) * FIN + 1)
                sp.dma_start(rows(out_b)[:, bass.ds(s * IT, IT), :],
                             att[:, :, :].rearrange("p (t h) d -> p t (h d)", t=IT)).then_inc(out_stored, 16)

            with sp.Fori(0, B - 1) as b:
                with sp.Fori(0, NS) as s:
                    store(b * NS + s, s, out[b])
                sp.dma_start(xs[:, :, :], rows(x1[b + 1])).then_inc(x_loaded, 16)
            with sp.Fori(0, NS) as s:
                store((B - 1) * NS + s, s, out[B - 1])
            sp.wait_ge(out_stored, 16 * B * NS + 1)

        @block.gpsimd
        def _(pool):
            pool.dma_start(mask16[:, :, :], mask_dram).then_inc(mask_loaded, 16)
            pool.sem_inc(out_stored, 1)
            nc.gpsimd.memset(pool_cell[:, :], 0.0)
            nc.gpsimd.memset(lift[:, :], LIFT)
            nc.gpsimd.memset(zero[:, :], 0.0)
            nc.gpsimd.memset(neg_half1[:, :], -0.5)
            nc.gpsimd.memset(eps1[:, :], EPS)
            nc.gpsimd.memset(neg_one[:, :], -1.0)
            nc.gpsimd.memset(ident1[:, :], 0.0).then_inc(consts_ready, 1)
            pool.wait_ge(consts_ready, 1)
            nc.gpsimd.affine_select(out=ident1[:, :], in_=ident1[:, :], compare_op=ALU.not_equal, fill=1.0,
                                    base=0, pattern=[[-1, P]], channel_multiplier=1).then_inc(consts_ready, 1)
            with pool.Fori(0, B) as b:
                pool.wait_ge(moments_done, b + 1)
                nc.gpsimd.tensor_tensor(rstd[:, :], moments[:, :, 1], eps1[:, :], ALU.add).then_inc(var_eps_done, 1)
                pool.wait_ge(var_eps_done, b + 1)
                nc.gpsimd.tensor_tensor(rstd[:, :], rstd[:, :], neg_half1[:, :], ALU.pow).then_inc(rstd_done, 1)
                pool.wait_ge(d_max_done, b + 1)
                pool_gate(nc, pool_cell)
                nc.gpsimd.partition_all_reduce(d_top[:, :], d_max[:, :], P, RMAX).then_inc(d_top_done, 1)
                pool.wait_ge(ab_done, b + 1)
                for k in range(GROUPS):
                    if k:
                        pool.wait_ge(wv_low_done, b * GROUPS + k)
                    tiles = slice(k * GT, (k + 1) * GT)
                    q = q_s[:, tiles, 0:F].rearrange("p t (h d) -> p t h d", h=H)
                    for first, weight in ((0, b_big), (E1, b_small)):
                        last = nc.gpsimd.tensor_tensor(wv[:, :, :, first:first + D], q,
                                                       weight[:, tiles, :].unsqueeze(3).to_broadcast([P, GT, H, D]), ALU.mult)
                    last.then_inc(wv_q_done, 1)
                with pool.Fori(0, NS) as s:
                    g = b * NS + s
                    pool.wait_ge(side_free, 2 + b * SIDE_USES + PRE_USES + (s + 1) * IT)
                    pool.wait_ge(sums_free, IT + (g + 1) * IT * H)
                    flat = lambda v: v[:, :, :, :].rearrange("p t h e -> p (t h) e")
                    rows_small = a_small[:, bass.ds(s * IT, IT), :].unsqueeze(3).to_broadcast([P, IT, H, E1])

                    def step(k, dst, x_, y_, op):
                        if k:
                            pool.wait_ge(fin_chain, g * FIN + k + 1)
                        nc.gpsimd.tensor_tensor(dst, x_, y_, op).then_inc(fin_chain, 1)

                    step(0, side_s[:, :, :, :], side_s[:, :, :, :], rows_small, ALU.mult)
                    step(1, flat(side_s), flat(side_s), flat(small_s), ALU.subtract)
                    step(2, flat(side_s), flat(side_s), flat(big_s), ALU.add)
                    step(3, recip[:, :], flat(side_s)[:, :, D], neg_one[:, :], ALU.pow)
                    pool.wait_ge(out_stored, g * 16 + 1)
                    step(4, att[:, :, :], flat(side_s)[:, :, 0:D], recip[:, :].unsqueeze(2).to_broadcast([P, IT * H, D]),
                         ALU.mult)
                    pool.wait_ge(elu_done, g + 1)
                    pool_gate(nc, pool_cell)
                    nc.gpsimd.tensor_scalar(e_att[:, :, :], e_att[:, :, :], -1.0, 0.0, ALU.add, ALU.min).then_inc(fin_chain, 1)
                    step(6, att[:, :, :], r_att[:, :, :], e_att[:, :, :], ALU.add)
                    step(7, att[:, :, :].rearrange("p (t h) d -> p t (h d)", t=IT),
                         att[:, :, :].rearrange("p (t h) d -> p t (h d)", t=IT), xs[:, bass.ds(s * IT, IT), :], ALU.add)

        @block.tensor
        def _(pe):
            pe.wait_ge(consts_ready, 2)
            pe.wait_ge(w_ready, 2)
            pe.wait_ge(mask_loaded, 16)
            pe.sem_inc(u_ready, 1)

            def fill(use):
                pe.wait_ge(side_free, use + 1)

            with pe.Fori(0, B) as b:
                u0 = b * SIDE_USES
                for t in range(NT):
                    pe.wait_ge(norm_done, b * NT + t + 1)
                    fill(u0 + t)
                    for c in range(KC):
                        last = nc.tensor.transpose(side[t % 2][:, c * P:(c + 1) * P], norm[:, t % 2, c * P:(c + 1) * P],
                                                   ident1[:, :])
                    last.then_inc(side_filled, 1)
                for t in range(NT):
                    if t == 0:
                        pe.wait_ge(side_free, u0 + NT + 2)
                    fill(u0 + NT + t)
                    for c in range(KC):
                        last = nc.tensor.matmul(side[t % 2][:, 0:WIDE], h_t[:, c, t * P:(t + 1) * P], w_s[:, c, :],
                                                start=(c == 0), stop=(c == KC - 1))
                        if t == NT - 1 and c == 0:
                            last.then_inc(u_used, UBUF)
                    last.then_inc(side_filled, 1)
                with pe.Fori(0, NS) as s:
                    n0 = (b * NS + s) * H

                    def score_rows(h):
                        pe.wait_ge(u_ready, (n0 + max(h - 1, 0)) * NT + 1)
                        for c in range(KC):
                            last = nc.tensor.matmul(s_rows[h % 2][:, :], w_src_neg[:, c, h, :], h_t[:, c, bass.ds(s * STRIP, STRIP)],
                                                    start=(c == 0), stop=(c == KC - 1))
                        last.then_inc(s_rows_filled, 1)

                    score_rows(0)
                    for h in range(H):
                        for j in range(NT):
                            if h == 0 and j == 0:
                                pe.wait_ge(wv_low_done, (b + 1) * GROUPS)
                            if j == 0:
                                fill(u0 + PRE_USES + s * IT + h)
                            for part in range(2):
                                last = nc.tensor.matmul(side[h % 2][:, 0:H * E1],
                                                        mask16[:, j, bass.ds(s * STRIP + h * P, P)],
                                                        wv16[:, j, part, :, E1:VW],
                                                        start=(j == 0 and part == 0), stop=(j == NT - 1 and part == 1))
                            if j == NT - 1:
                                last.then_inc(side_filled, 1)
                            if j == 4 and h + 1 < H:
                                score_rows(h + 1)
                            pe.wait_ge(u_ready, (n0 + h) * NT + j + 2)
                            for q in range(IT):
                                if j == 0:
                                    pe.wait_ge(sums_free, (n0 + h) * IT + q + 1)
                                for part in range(2):
                                    last = nc.tensor.matmul(sums[q][:, 0:VW], u[:, j % UBUF, q * P:(q + 1) * P],
                                                            wv16[:, j, part, h, :],
                                                            start=(j == 0 and part == 0), stop=(j == NT - 1 and part == 1))
                            last.then_inc(u_used, 1)

        @block.scalar
        def _(act):
            act.wait_ge(consts_ready, 2)
            act.wait_ge(w_ready, 1)
            for c in range(KC):
                last = nc.scalar.activation(w_src_neg[:, c, :, :], w_s[:, c, F:F + H].unsqueeze(2).to_broadcast([P, H, P]),
                                            ACT.Copy, scale=-1.0)
            last.then_inc(w_ready, 1)
            act.sem_inc(fin_chain, 1)
            act.wait_ge(w_ready, 2)
            nc.scalar.activation(e_att[:, 0, 0:1], lift[:, :], ACT.Copy).then_inc(side_free, 2)
            nc.scalar.activation(e_att[:, 0, 1:2], lift[:, :], ACT.Copy).then_inc(sums_free, IT)
            with act.Fori(0, B) as b:
                u0 = b * SIDE_USES
                for t in range(NT):
                    act.wait_ge(side_filled, u0 + t + 1)
                    nc.scalar.activation(h_t[:, :, t * P:(t + 1) * P],
                                         side[t % 2][:, 0:F].rearrange("p (c n) -> p c n", c=KC), ACT.Relu).then_inc(side_free, 1)
                for t in range(NT):
                    act.wait_ge(side_filled, u0 + NT + t + 1)
                    nc.scalar.activation(q_s[:, t, :], side[t % 2][:, 0:WIDE], ACT.Copy).then_inc(side_free, 1)
                act.wait_ge(zd_done, b + 1)
                act.wait_ge(z_parts_done, b + 1)
                nc.scalar.activation(b_big[:, :, :], d_rel[:, :, :], ACT.Exp, bias=lift[:, 0:1])
                nc.scalar.activation(b_small[:, :, :], d_rel[:, :, :], ACT.Exp, bias=lift[:, 0:1], scale=0.2)
                nc.scalar.activation(a_big[:, :, :], z_neg[:, :, :], ACT.Exp, bias=zero[:, 0:1], scale=0.8)
                nc.scalar.activation(a_small[:, :, :], z_pos[:, :, :], ACT.Exp, bias=zero[:, 0:1], scale=-0.8).then_inc(ab_done, 1)
                act.wait_ge(ab_done, b + 1)
                for k in range(GROUPS):
                    tiles = slice(k * GT, (k + 1) * GT)
                    if k:
                        act.wait_ge(wv_low_done, b * GROUPS + k)
                    nc.scalar.activation(wv[:, :, :, D], b_big[:, tiles, :], ACT.Copy)
                    nc.scalar.activation(wv[:, :, :, VW - 1], b_small[:, tiles, :], ACT.Copy).then_inc(wv_b_done, 1)
                    act.wait_ge(wv_b_done, b * GROUPS + k + 1)
                    act.wait_ge(wv_q_done, b * GROUPS + k + 1)
                    nc.scalar.activation(wv16[:, tiles, 0, :, :].rearrange("p t h e -> p t (h e)"),
                                         wv[:, :, :, :].rearrange("p t h e -> p t (h e)"), ACT.Copy).then_inc(wv_high_done, 1)
                with act.Fori(0, NS) as s:
                    g = b * NS + s
                    act.wait_ge(fin_chain, g * FIN + 1)
                    for h in range(H):
                        act.wait_ge(u_used, b * U_BATCH + UBUF + (s * H + h + 1) * NT)
                        for q in range(IT):
                            rows_of = lambda v: v[:, bass.ds(s * IT + q, 1), h]
                            nc.scalar.activation(big_s[:, q, h, :], sums[q][:, 0:E1], ACT.Copy, scale=rows_of(a_big))
                            nc.scalar.activation(small_s[:, q, h, :], sums[q][:, E1:VW], ACT.Copy, scale=rows_of(a_small))\
                                .then_inc(sums_free, 1)
                        act.wait_ge(side_filled, u0 + PRE_USES + s * IT + h + 1)
                        nc.scalar.activation(side_s[:, h, :, :].rearrange("p h e -> p (h e)"), side[h % 2][:, 0:H * E1],
                                             ACT.Copy).then_inc(side_free, 1)
                    act.wait_ge(fin_chain, g * FIN + 6)
                    nc.scalar.activation(e_att[:, :, :], att[:, :, :], ACT.Exp, bias=zero[:, 0:1])
                    nc.scalar.activation(r_att[:, :, :], att[:, :, :], ACT.Relu).then_inc(elu_done, 1)

        @block.vector
        def _(dve):
            dve.wait_ge(mask_loaded, 16)
            dve.wait_ge(consts_loaded, 16 * len(consts))
            for k in range(2):
                for c in range(KC):
                    last = nc.vector.tensor_tensor(wa[:, k, c, :, :], w_s[:, c, 0:F].rearrange("p (h d) -> p h d", h=H),
                                                   a_s[:, k, :].unsqueeze(1).to_broadcast([P, H, D]), ALU.mult)
            last.then_inc(w_chain, 1)
            dve.wait_ge(w_chain, 1)
            for k in range(2):
                for c in range(KC):
                    last = nc.vector.tensor_reduce(w_s[:, c, F + k * H:F + (k + 1) * H], wa[:, k, c, :, :], AX.X, ALU.add)
            last.then_inc(w_ready, 1)
            with dve.Fori(0, B) as b:
                u0 = b * SIDE_USES
                dve.wait_ge(x_loaded, (b + 1) * 16)
                for t in range(NT):
                    last = nc.vector.bn_stats(stats[:, t, :], xs[:, t, :])
                last.then_inc(stats_done, 1)
                dve.wait_ge(stats_done, b + 1)
                dve_gate(nc, dve_cell)
                for t in range(NT):
                    last = nc.vector.bn_aggr(moments[:, t, :], stats[:, t, :])
                last.then_inc(moments_done, 1)
                dve.wait_ge(moments_done, b + 1)
                dve.wait_ge(rstd_done, b + 1)
                for t in range(NT):
                    if t >= 2:
                        dve.wait_ge(side_filled, u0 + t - 1)
                    nc.vector.tensor_scalar(norm[:, t % 2, :], xs[:, t, :], moments[:, t, 0:1], rstd[:, t:t + 1],
                                            ALU.subtract, ALU.mult).then_inc(norm_done, 1)
                dve.wait_ge(side_free, 2 + u0 + PRE_USES)
                nc.vector.tensor_reduce(d_max[:, :], q_s[:, :, F + H:WIDE].rearrange("p t h -> p h t"), AX.X, ALU.max)\
                    .then_inc(d_max_done, 1)
                dve.wait_ge(d_top_done, b + 1)
                top = d_top[:, :].unsqueeze(1).to_broadcast([P, NT, H])
                nc.vector.tensor_tensor(z[:, :, :], q_s[:, :, F:F + H], top, ALU.add)
                nc.vector.tensor_tensor(d_rel[:, :, :], q_s[:, :, F + H:WIDE], top, ALU.subtract).then_inc(zd_done, 1)
                dve.wait_ge(zd_done, b + 1)
                nc.vector.tensor_scalar(z_neg[:, :, :], z[:, :, :], 0.0, None, ALU.min)
                nc.vector.tensor_scalar(z_pos[:, :, :], z[:, :, :], 0.0, None, ALU.max).then_inc(z_parts_done, 1)
                for k in range(GROUPS):
                    dve.wait_ge(wv_high_done, b * GROUPS + k + 1)
                    tiles = slice(k * GT, (k + 1) * GT)
                    flat = lambda v: v.rearrange("p t h e -> p t (h e)")
                    nc.vector.tensor_tensor(flat(wv16[:, tiles, 1, :, :]), flat(wv[:, :, :, :]), flat(wv16[:, tiles, 0, :, :]),
                                            ALU.subtract).then_inc(wv_low_done, 1)
                with dve.Fori(0, NS) as s:
                    g = b * NS + s
                    for h in range(H):
                        n = g * H + h
                        dve.wait_ge(s_rows_filled, n + 1)
                        for j in range(NT):
                            dve.wait_ge(u_used, b * U_BATCH + (s * H + h) * NT + j + 1)
                            nc.vector.scalar_tensor_tensor(u[:, j % UBUF, :], s_rows[h % 2][:, :],
                                                           q_s[:, j, F + H + h:F + H + h + 1],
                                                           mask16[:, j, bass.ds(s * STRIP, STRIP)],
                                                           ALU.is_le, ALU.mult).then_inc(u_ready, 1)


_INS = ["x", "adj", "L0_gnn_Wq", "L0_gnn_bq", "L0_gnn_Wk", "L0_gnn_bk", "L0_gnn_Wv", "L0_gnn_bv",
        "L0_gnn_Wo", "L0_gnn_bo", "L0_gnn_gamma", "L0_gnn_beta", "L1_gnn_W", "L1_gnn_a"]


def build(nc, x, adj, wq_t, bq, wk_t, bk, wv_t, bv, wo_t, bo, gamma, beta, w, a, out):
    x1 = nc.dram_tensor("x1", [B, N, F], F32).ap()
    mask_dram = nc.dram_tensor("mask_t", [P, NT, N], U8).ap()
    with nc.sbuf_tensor("mask8", [P, NT, N], U8) as mask8:
        with nc.sbuf_tensor("ident16", [P, P], F16) as ident16:
            mask_block(nc, adj, ident16, mask8, mask_dram)
        layer0_block(nc, x, wq_t, bq, wk_t, bk, wv_t, bv, wo_t, bo, gamma, beta, x1, mask8)
    layer1_block(nc, x1, w, a, out, mask_dram)


def kernel(**inputs):
    import numpy as np
    import concourse.bacc as bacc
    from concourse.bass_utils import run_bass_kernel_spmd

    nc = bacc.Bacc("TRN2", target_bir_lowering=False, num_devices=1)
    arrays, args = {}, []
    for name in _INS:
        a = np.asarray(inputs[name])
        a = np.ascontiguousarray(a.T if name in ("L0_gnn_Wq", "L0_gnn_Wk", "L0_gnn_Wv", "L0_gnn_Wo") else a)
        if name in ("L0_gnn_bq", "L0_gnn_bk"):
            a = np.ascontiguousarray(a.reshape(H, D).T)
        arrays[f"in_{name}"] = a
        args.append(nc.dram_tensor(f"in_{name}", a.shape, mybir.dt.from_np(a.dtype), kind="ExternalInput").ap())
    args.append(nc.dram_tensor("out", [B, N, F], F32, kind="ExternalOutput").ap())
    build(nc, *args)
    r = run_bass_kernel_spmd(nc, [arrays], core_ids=[0])
    return np.asarray(r.results[0]["out"])
```
